# Optimizing a Trainium2 kernel written in Bass

```python
import numpy as np
import jax
import jax.numpy as jnp

def _softmax(x, axis=-1):
    return jax.nn.softmax(x, axis=axis)
def _gelu(x):
    return jax.nn.gelu(x, approximate=True)
def _silu(x):
    return jax.nn.silu(x)
def _sigmoid(x):
    return jax.nn.sigmoid(x)
def _layernorm(x, axis=-1, eps=1e-5):
    m = jnp.mean(x, axis=axis, keepdims=True)
    v = jnp.var(x, axis=axis, keepdims=True)
    return (x - m) / jnp.sqrt(v + eps)
def _scatter_add(tgt, idx, src, axis=0):
    return tgt.at[idx].add(src)
def _segment_sum(src, seg, n):
    return jax.ops.segment_sum(src, seg, n)

kernel_name = 'mk_conv_preact_d1_conv_nchw128_cfd58e'

def setup_inputs(seed: int = 0):
    np.random.seed(seed)
    _w = jnp.asarray
    def _rec_inputs():
        import jax
        import jax.numpy as jnp
        _gk = jax.random.key(seed)
        x = -0.0003929 + 0.9999 * jax.random.normal(jax.random.fold_in(_gk, 1), (2, 128, 256, 256), jnp.float32)
        return x
    x = _rec_inputs()
    def _L0_conv_setup():
        import jax, jax.numpy as jnp
        import numpy as np
        BS = 4
        NH = 8
        DH = 32
        DIN = 128
        DOUT = 128
        H = 256
        W = 256
        B = 2
        key = jax.random.key(seed)
        k1, k2, k3 = jax.random.split(key, 3)
        x = jax.random.normal(k1, (B, DIN, H, W), jnp.float32)
        w_in = jax.random.normal(k2, (3 * NH * DH, DIN), jnp.float32) * 0.05
        b_in = jnp.full((3 * NH * DH,), 0.01, jnp.float32)
        w_out = jax.random.normal(k3, (DOUT, NH * DH), jnp.float32) * 0.05
        b_out = jnp.full((DOUT,), 0.01, jnp.float32)
        d = jnp.abs(jnp.arange(4 * BS, dtype=jnp.float32) - 2 * BS) ** 2.0
        vals = 1.0 / 16.0 * (d[:, None] + d[None, :]).reshape(-1)
        pce = jnp.tile(vals[None, :], (NH, 1)).astype(jnp.float32)
        return {'x': x, 'w_in': w_in, 'b_in': b_in, 'w_out': w_out, 'b_out': b_out, 'pce': pce}
    _L0_conv_all = _L0_conv_setup()
    _L0_conv_in = {k: v for k, v in _L0_conv_all.items() if k in ('w_in', 'b_in', 'w_out', 'b_out', 'pce', )}
    del _L0_conv_all

    return {
        "x": x,
        "L0_conv_w_in": _L0_conv_in["w_in"],
        "L0_conv_b_in": _L0_conv_in["b_in"],
        "L0_conv_w_out": _L0_conv_in["w_out"],
        "L0_conv_b_out": _L0_conv_in["b_out"],
        "L0_conv_pce": _L0_conv_in["pce"],
    }

def reference(x, L0_conv_w_in, L0_conv_b_in, L0_conv_w_out, L0_conv_b_out, L0_conv_pce):
    import jax
    import jax.numpy as jnp
    def _L0_conv_ref(x, w_in, b_in, w_out, b_out, pce):
        import jax, jax.numpy as jnp
        import numpy as np
        BS = 4
        NH = 8
        DH = 32
        DIN = 128
        DOUT = 128
        H = 256
        W = 256
        B = 2
        Bx, din, Hx, Wx = x.shape
        hb = Wx // BS
        vb = Hx // BS
        xt = jnp.swapaxes(x, 1, 3)
        xt = xt.reshape(Bx, hb, BS, vb, BS, din).transpose(0, 1, 3, 2, 4, 5)
        proj = xt @ w_in.T + b_in
        q = proj[..., :NH * DH]
        kv = proj[..., NH * DH:]
        kv = jnp.pad(kv, ((0, 0), (1, 1), (1, 1), (0, 0), (0, 0), (0, 0)))
        kv = jnp.concatenate((kv[:, :-2], kv[:, 1:-1], kv[:, 2:]), axis=3)
        kv = jnp.concatenate((kv[:, :, :-2], kv[:, :, 1:-1], kv[:, :, 2:]), axis=4)
        q = q.reshape(Bx, hb, vb, BS * BS, NH, DH).swapaxes(3, 4)
        k = kv[..., :NH * DH].reshape(Bx, hb, vb, 9 * BS * BS, NH, DH).swapaxes(3, 4)
        v = kv[..., NH * DH:].reshape(Bx, hb, vb, 9 * BS * BS, NH, DH).swapaxes(3, 4)
        a0 = jnp.arange(BS)
        a1 = jnp.arange(3 * BS)
        net = a1[None, :] + BS - a0[:, None]
        idx = (4 * BS * net)[:, None, :, None] + net[None, :, None, :]
        idx = idx.reshape(BS * BS, 9 * BS * BS)
        bias = pce[:, idx]
        ex = jnp.zeros((hb, 3 * BS), bool).at[0, :BS].set(True).at[-1, 2 * BS:].set(True)
        ey = jnp.zeros((vb, 3 * BS), bool).at[0, :BS].set(True).at[-1, 2 * BS:].set(True)
        blocked = ex[:, None, :, None] | ey[None, :, None, :]
        cut = jnp.where(blocked, jnp.inf, 0.0).reshape(hb, vb, 1, 1, 9 * BS * BS)
        amask = -(bias[None, None] + cut)
        scale = 1.0 / jnp.sqrt(jnp.float32(DH))
        scores = jnp.einsum('bhvnqd,bhvnkd->bhvnqk', q, k) * scale + amask
        attn = jax.nn.softmax(scores, axis=-1)
        out = jnp.einsum('bhvnqk,bhvnkd->bhvnqd', attn, v)
        out = out.swapaxes(3, 4).reshape(Bx, hb, vb, BS * BS, NH * DH)
        out = out @ w_out.T + b_out
        out = out.reshape(Bx, hb, vb, BS, BS, DOUT).swapaxes(2, 3).reshape(Bx, Wx, Hx, DOUT)
        return jnp.swapaxes(out, 1, 3)

    def _gn(v, G=32, eps=1e-5):
        B_, C_, H_, W_ = v.shape
        g = v.reshape(B_, G, C_ // G, H_, W_)
        m = jnp.mean(g, axis=(2, 3, 4), keepdims=True)
        s = jnp.var(g, axis=(2, 3, 4), keepdims=True)
        return ((g - m) / jnp.sqrt(s + eps)).reshape(v.shape)

    def _ln_c(v, eps=1e-6):
        m = jnp.mean(v, axis=1, keepdims=True)
        s = jnp.var(v, axis=1, keepdims=True)
        return (v - m) / jnp.sqrt(s + eps)

    def _ln_t(v, eps=1e-5):
        m = jnp.mean(v, axis=-1, keepdims=True)
        s = jnp.var(v, axis=-1, keepdims=True)
        return (v - m) / jnp.sqrt(s + eps)

    def _to_tokens(v):
        B_, C_, H_, W_ = v.shape
        return v.reshape(B_, C_, H_ * W_).transpose(0, 2, 1)
    def _from_tokens(t, like):
        B_, C_, H_, W_ = like.shape
        return t.transpose(0, 2, 1).reshape(B_, C_, H_, W_)

    x = x + _L0_conv_ref(_gn(x), L0_conv_w_in, L0_conv_b_in, L0_conv_w_out, L0_conv_b_out, L0_conv_pce)
    return x


_drawn_inputs = setup_inputs


def setup_inputs(seed=0):
    import zlib

    import numpy as np

    out = dict(_drawn_inputs(seed))
    spreads = {'L0_conv_b_in': (0.009999999776482582, 0.2), 'L0_conv_b_out': (0.009999999776482582, 0.2)}
    factors = {}
    for name, (base, spread) in spreads.items():
        noise = np.random.default_rng([zlib.crc32(name.encode()), seed]).standard_normal(out[name].shape)
        drawn = base * np.exp(spread * noise) if base else spread * noise
        out[name] = jnp.asarray(drawn.astype(out[name].dtype))
    for name, factor in factors.items():
        out[name] = (out[name] * factor).astype(out[name].dtype)
    return out
```

```python
from contextlib import ExitStack

import concourse.bass as bass
from concourse import mybir
from concourse.alu_op_type import AluOpType as ALU

BATCH, CH, HEIGHT, WIDTH = 2, 128, 256, 256
HEADS, HEAD_DIM, BLOCK = 8, 32, 4
GROUP_CH = 4
EPS = 1e-5
SCALE = HEAD_DIM ** -0.5
PARTS = 128
HG = 2
HPG = HEADS // HG
QB = BLOCK * BLOCK
WIN = 3 * BLOCK
STRIP = 2 * BLOCK
KROWS = STRIP + 2 * BLOCK
STRIPS = HEIGHT // STRIP
ALL_STRIPS = BATCH * STRIPS
QUADS = WIDTH // (4 * BLOCK)
STEPS = QUADS + 1
SPAN = 4 * BLOCK
PAD = 3 * BLOCK
XCOLS = STEPS * SPAN
BLOCKED = 1.0e30
BIG = 3.0e38
STAT_ROWS = 16
STAT_LOADS = HEIGHT // STAT_ROWS
STAT_PIECE = 512
STAT_PIECES = STAT_ROWS * WIDTH // STAT_PIECE


def build(nc, x, w_in_t, b_in_c, b_q_r, w_out_t, b_out_c, pce, ident_d, group_avg_d, head_mask_d, out):
    f32 = mybir.dt.float32
    ACT = mybir.ActivationFunctionType

    ctx = ExitStack()
    with ctx:
        def sb(name, shape):
            return ctx.enter_context(nc.sbuf_tensor(name, shape, f32))

        def pb(name):
            return ctx.enter_context(nc.psum_tensor(name, [PARTS, 512], f32))

        def sem(name):
            return ctx.enter_context(nc.semaphore(name))

        w_in = sb("w_in", [PARTS, 3 * HEADS * HEAD_DIM])
        w_out = sb("w_out", [PARTS, HG, CH])
        b_in = sb("b_in", [PARTS, 3 * HG])
        b_q = sb("b_q", [1, HG * PARTS])
        b_out = sb("b_out", [PARTS, 1])
        ident = sb("ident", [PARTS, PARTS])
        group_avg = sb("group_avg", [PARTS, PARTS])
        head_mask = sb("head_mask", [PARTS, HPG])
        stats = sb("stats", [PARTS, BATCH * STAT_LOADS * STAT_PIECES, 6])
        stat_in = sb("stat_in", [PARTS, 2, STAT_ROWS * WIDTH])
        moments = sb("moments", [PARTS, BATCH, 2])
        var_eps = sb("var_eps", [PARTS, BATCH])
        minus_half = sb("minus_half", [PARTS, BATCH])
        norm_all = sb("norm_all", [PARTS, BATCH, 2])
        norm_now = sb("norm_now", [PARTS, 2])
        bias_raw = sb("bias_raw", [PARTS, WIN, WIN])
        bias_all = sb("bias_all", [PARTS, 2, 2, 3, WIN, WIN])
        bias_now = sb("bias_now", [PARTS, 2, 3, WIN, WIN])
        x_strip = sb("x_strip", [PARTS, 2, KROWS, XCOLS])
        y_strip = sb("y_strip", [PARTS, STRIP, WIDTH])
        ones = sb("ones", [1, PARTS])
        xh = sb("xh", [PARTS, 2, SPAN, KROWS])
        k_win = sb("k_win", [PARTS, 2, HG, 6 * BLOCK, KROWS])
        v_sb = sb("v_sb", [PARTS, 2, 2, HEADS * HEAD_DIM])
        q_diag = sb("q_diag", [PARTS, 2, HG, 2, 4, HPG * QB])
        probs = sb("probs", [PARTS, 2, 4, 2, 4 * BLOCK, KROWS])
        minus_max = sb("minus_max", [PARTS, 2, 8])
        row_sum = sb("row_sum", [PARTS, 2, 8])
        inv_sum = sb("inv_sum", [PARTS, 2, 8])
        pt_sb = sb("pt_sb", [PARTS, 2, 4, 2, 2, PARTS])
        o_sb = sb("o_sb", [PARTS, HG, 8 * QB])

        k_bank, v_bank, q_bank, o_bank = pb("k_bank"), pb("v_bank"), pb("q_bank"), pb("o_bank")
        s_bank = [pb("s_bank0"), pb("s_bank1")]
        t_bank = [pb("t_bank0"), pb("t_bank1")]

        loaded_const = sem("loaded_const")
        bias_in = sem("bias_in")
        stat_loaded = [sem("stat_loaded0"), sem("stat_loaded1")]
        stat_read = [sem("stat_read0"), sem("stat_read1")]
        dve_step = sem("dve_step")
        avg_in, avg_out, var_ready, rstd_ready = sem("avg_in"), sem("avg_out"), sem("var_ready"), sem("rstd_ready")
        cleared_pool = sem("cleared_pool")
        cleared_dve = sem("cleared_dve")
        x_loaded = sem("x_loaded")
        y_stored = sem("y_stored")
        xh_ready = sem("xh_ready")
        k_made, k_ready, k_carried = sem("k_made"), sem("k_ready"), sem("k_carried")
        q_made, q_ready = sem("q_made"), sem("q_ready")
        v_made, v_ready = sem("v_made"), sem("v_ready")
        s_made = sem("s_made")
        biased = sem("biased")
        exp_done = sem("exp_done")
        inverted = sem("inverted")
        normed = sem("normed")
        t_made = sem("t_made")
        pt_act, pt_dve = sem("pt_act"), sem("pt_dve")
        o_made, o_ready, y_made, y_ready = sem("o_made"), sem("o_ready"), sem("y_made"), sem("y_ready")

        N_CONST = 8
        N_BIAS = QB

        def step_no(G, u):
            return G * STEPS + u

        def quad_no(G, t):
            return G * QUADS + t

        def over_strip(eng, G, prologue, body, drain):
            prologue(G)
            body(G, 0, 0)
            with eng.Fori(0, QUADS // 2 - 1) as k:
                body(G, k * 2 + 1, 1)
                body(G, k * 2 + 2, 0)
            body(G, QUADS - 1, 1)
            drain(G)

        def window(par, i, r):
            return probs[:, par, i, r, BLOCK * (i % 2):BLOCK * (i % 2) + WIN, BLOCK * r:BLOCK * r + WIN]

        first = lambda t: isinstance(t, int) and t == 0
        last = lambda t: isinstance(t, int) and t == QUADS - 1

        block = ctx.enter_context(nc.Block())

        @block.sync
        def _(sp):
            for dst, src in ((w_in[:], w_in_t), (w_out[:], w_out_t), (b_in[:], b_in_c), (b_q[:], b_q_r),
                             (b_out[:], b_out_c),
                             (ident[:], ident_d), (group_avg[:], group_avg_d), (head_mask[:], head_mask_d)):
                sp.dma_start(dst, src).then_inc(loaded_const, 16)
            for b in range(BATCH):
                with sp.Fori(0, STAT_LOADS // 2) as n:
                    for par in range(2):
                        sp.wait_ge(stat_read[par], n + b * STAT_LOADS // 2)
                        src = x[b, :, bass.ds((n * 2 + par) * STAT_ROWS, STAT_ROWS), :]
                        sp.dma_start(stat_in[:, par, :], src.rearrange("c h w -> c (h w)")).then_inc(stat_loaded[par], 16)

            def load(G, b, row0, rows, to_row):
                sp.wait_ge(x_loaded, G * 16)
                sp.dma_start(x_strip[:, bass.ds(G % 2, 1), to_row:to_row + rows, PAD:PAD + WIDTH]
                             .rearrange("c a h w -> c (a h) w"),
                             x[b, :, bass.ds(row0, rows), :]).then_inc(x_loaded, 16)

            def store(G, b, g):
                sp.wait_ge(y_ready, quad_no(G + 1, 0))
                sp.dma_start(out[b, :, bass.ds(g * STRIP, STRIP), :].rearrange("c h w -> c (h w)"),
                             y_strip[:].rearrange("c h w -> c (h w)")).then_inc(y_stored, 16)

            sp.wait_ge(cleared_pool, 1)
            load(0, 0, 0, KROWS - BLOCK, BLOCK)
            for b in range(BATCH):
                base = b * STRIPS
                with sp.Fori(0, STRIPS - 2) as g:
                    sp.wait_ge(y_ready, quad_no(g + base, 0))
                    load(g + (base + 1), b, g * STRIP + (STRIP - BLOCK), KROWS, 0)
                    store(g + base, b, g)
                sp.wait_ge(y_ready, quad_no(base + STRIPS - 2, 0))
                load(base + STRIPS - 1, b, HEIGHT - KROWS + BLOCK, KROWS - BLOCK, 0)
                store(base + STRIPS - 2, b, STRIPS - 2)
                if b + 1 < BATCH:
                    sp.wait_ge(y_ready, quad_no(base + STRIPS - 1, 0))
                    load(base + STRIPS, b + 1, 0, KROWS - BLOCK, BLOCK)
                store(base + STRIPS - 1, b, STRIPS - 1)
            sp.wait_ge(y_stored, 16 * ALL_STRIPS)

        @block.tensor
        def _(pe):
            pe.wait_ge(loaded_const, 16 * N_CONST)
            pe.wait_ge(cleared_pool, 3)
            pe.wait_ge(avg_in, 1)
            nc.tensor.matmul(o_bank[:, 0:2 * BATCH], group_avg[:], moments[:].rearrange("p b m -> p (b m)"),
                             start=True, stop=True).then_inc(avg_out, 1)

            def project_k(G, u, par):
                U = step_no(G, u)
                pe.wait_ge(xh_ready, U + 1)
                pe.wait_ge(k_ready, U)
                for g in range(HG):
                    c0 = (HG + g) * PARTS
                    mm = nc.tensor.matmul(k_bank[:, g * 256:(g + 1) * 256], w_in[:, c0:c0 + PARTS],
                                          xh[:, par].rearrange("p h w -> p (h w)"), start=True, stop=True)
                mm.then_inc(k_made, 1)

            def project_q(G, u, par):
                pe.wait_ge(q_ready, step_no(G, u))
                for g in range(HG):
                    bank = q_bank[:, g * 128:(g + 1) * 128]
                    xq = xh[:, par, :, BLOCK:BLOCK + STRIP].rearrange("p w (r h) -> p r w h", h=BLOCK)
                    nc.tensor.matmul(bank, w_in[:, g * PARTS:(g + 1) * PARTS], xq, start=True, stop=False)
                    mm = nc.tensor.matmul(bank, b_q[:, g * PARTS:(g + 1) * PARTS], ones[:], start=False, stop=True)
                mm.then_inc(q_made, 1)

            def project_v(G, u, par):
                pe.wait_ge(v_ready, step_no(G, u))
                for c in range(2):
                    mm = nc.tensor.matmul(v_bank[:, c * 256:(c + 1) * 256],
                                          xh[:, par, c * 8:(c + 1) * 8, :].rearrange("p w h -> p (w h)"),
                                          w_in[:, 2 * HG * PARTS:], start=True, stop=True)
                mm.then_inc(v_made, 1)

            def scores(G, t, par, i):
                J = quad_no(G, t)
                if i == 0:
                    pe.wait_ge(k_ready, step_no(G, t) + 2)
                    pe.wait_ge(k_carried, step_no(G, t) + 1)
                    pe.wait_ge(q_ready, step_no(G, t) + 2)
                pe.wait_ge(biased, J * 8 if first(t) and i < 2 else J * 8 + 2 * (i - 1))
                for r in range(2):
                    for g in range(HG):
                        mm = nc.tensor.matmul(
                            s_bank[i % 2][64 * g:64 * (g + 1), 144 * r:144 * (r + 1)],
                            q_diag[:, par, g, r, 3] if i == 0 else q_diag[:, 1 - par, g, r, i - 1],
                            k_win[:, par, g, BLOCK * i:BLOCK * i + WIN, BLOCK * r:BLOCK * r + WIN],
                            start=True, stop=True)
                mm.then_inc(s_made, 1)

            def transposes(G, t, par, i):
                J = quad_no(G, t)
                pe.wait_ge(normed, J * 8 + 2 * i + 2)
                pe.wait_ge(pt_act if i % 2 == 0 else pt_dve, J * 2 + i // 2)
                for r in range(2):
                    for slot in range(2):
                        half = 1 - slot if i < 2 else slot
                        mm = nc.tensor.transpose(t_bank[i % 2][:, (2 * r + slot) * 128:(2 * r + slot + 1) * 128],
                                                 probs[:, par, i, r, half * 8:(half + 1) * 8, :].rearrange("p w h -> p (w h)"),
                                                 ident[:])
                mm.then_inc(t_made, 1)

            def weigh_v(G, t, par):
                J = quad_no(G, t)
                pe.wait_ge(pt_act, J * 2 + 2)
                pe.wait_ge(pt_dve, J * 2 + 2)
                pe.wait_ge(v_ready, step_no(G, t) + 2)
                pe.wait_ge(y_ready, J)
                for g in range(HG):
                    for v, i0, i1, slot in ((v_sb[:, 1 - par, 0], 0, 4, 0), (v_sb[:, par, 1], 0, 2, 1),
                                            (v_sb[:, 1 - par, 1], 2, 4, 1)):
                        for h in range(HPG):
                            c0 = (g * HPG + h) * QB
                            p = pt_sb[:, par, i0:i1, :, slot, c0:c0 + QB].rearrange("p i r q -> p r i q")
                            o = o_bank[32 * h:32 * (h + 1), g * 128:(g + 1) * 128].rearrange("p (r i q) -> p r i q", r=2, i=4)
                            mm = nc.tensor.matmul(
                                o[:, :, i0:i1, :],
                                v[:, (g * HPG + h) * HEAD_DIM:(g * HPG + h + 1) * HEAD_DIM], p,
                                start=slot == 0, stop=i0 == 2)
                mm.then_inc(o_made, 1)

            def project_out(G, t, par):
                J = quad_no(G, t)
                pe.wait_ge(o_ready, J + 1)
                for g in range(HG):
                    o = o_sb[:, g].rearrange("p (r iw h) -> p r h iw", r=2, h=BLOCK)
                    mm = nc.tensor.matmul(o_bank[:, 256:384], w_out[:, g], o, start=g == 0, stop=g == HG - 1)
                mm.then_inc(y_made, 1)

            def prologue(G):
                for u in range(2):
                    project_k(G, u, u)
                    project_q(G, u, u)
                project_v(G, 0, 0)

            def body(G, t, par):
                for i in range(4):
                    scores(G, t, par, i)
                    if not first(t):
                        transposes(G, t - 1, 1 - par, i)
                    if i == 1 and not last(t):
                        project_k(G, t + 2, par)
                if not last(t):
                    project_q(G, t + 2, par)
                if not first(t):
                    weigh_v(G, t - 1, 1 - par)
                project_v(G, t + 1, 1 - par)
                if not first(t):
                    project_out(G, t - 1, 1 - par)

            def drain(G):
                for i in range(4):
                    transposes(G, QUADS - 1, 1, i)
                weigh_v(G, QUADS - 1, 1)
                project_out(G, QUADS - 1, 1)

            with pe.Fori(0, ALL_STRIPS) as G:
                over_strip(pe, G, prologue, body, drain)

        @block.scalar
        def _(act):
            for q in range(QB):
                ww, hh = q // BLOCK, q % BLOCK
                src = bass.AP(pce.tensor, 16 * (BLOCK - ww) + (BLOCK - hh), [[256, HEADS], [16, WIN], [1, WIN]])
                act.dma_start(bias_raw[q::QB], src).then_inc(bias_in, 16)

            act.wait_ge(loaded_const, 16 * N_CONST)

            def keep_k(G, u, par):
                U = step_no(G, u)
                act.wait_ge(k_made, U + 1)
                if isinstance(u, int) and u < 2:
                    act.wait_ge(s_made, G * (4 * QUADS))
                    act.wait_ge(k_carried, G * STEPS)
                else:
                    act.wait_ge(s_made, 4 * (quad_no(G, u) - 2))
                    act.wait_ge(k_carried, U - 1)
                for g in range(HG):
                    ins = nc.scalar.activation(
                        k_win[:, 1 - par, g, 2 * BLOCK:, :].rearrange("p w h -> p (w h)"),
                        k_bank[:, g * 256:(g + 1) * 256],
                        ACT.Identity, bias=b_in[:, HG + g:HG + g + 1])
                ins.then_inc(k_ready, 1)

            def exps(G, t, par, i):
                J = quad_no(G, t)
                for r in range(2):
                    n = 2 * i + r
                    act.wait_ge(biased, J * 8 + n + 1)
                    w = window(par, i, r)
                    nc.scalar.activation(w, w, ACT.Exp, bias=minus_max[:, par, n:n + 1], scale=-1.0,
                                         accum_out=row_sum[:, par, n:n + 1]).then_inc(exp_done, 1)

            def keep_pt(G, t, par, i):
                J = quad_no(G, t)
                act.wait_ge(t_made, J * 4 + i + 1)
                nc.scalar.activation(pt_sb[:, par, i].rearrange("p r s c -> p (r s c)"), t_bank[i % 2][:],
                                     ACT.Copy).then_inc(pt_act, 1)

            def keep_o(G, t):
                J = quad_no(G, t)
                act.wait_ge(o_made, J + 1)
                act.wait_ge(y_made, J)
                for g in range(HG):
                    ins = nc.scalar.activation(o_sb[:, g], o_bank[:, g * 128:(g + 1) * 128], ACT.Identity,
                                               bias=b_in[:, 2 * HG + g:2 * HG + g + 1])
                ins.then_inc(o_ready, 1)

            def prologue(G):
                for u in range(2):
                    keep_k(G, u, u)

            def body(G, t, par):
                exps(G, t, par, 0)
                if not first(t):
                    keep_pt(G, t - 1, 1 - par, 0)
                exps(G, t, par, 1)
                if not last(t):
                    keep_k(G, t + 2, par)
                exps(G, t, par, 2)
                if not first(t):
                    keep_pt(G, t - 1, 1 - par, 2)
                exps(G, t, par, 3)
                if not first(t):
                    keep_o(G, t - 1)

            def drain(G):
                keep_pt(G, QUADS - 1, 1, 0)
                keep_pt(G, QUADS - 1, 1, 2)
                keep_o(G, QUADS - 1)

            with act.Fori(0, ALL_STRIPS) as G:
                over_strip(act, G, prologue, body, drain)

        @block.gpsimd
        def _(pool):
            nc.gpsimd.memset(x_strip[:], 0.0).then_inc(cleared_pool, 1)
            nc.gpsimd.memset(minus_half[:], -0.5).then_inc(cleared_pool, 1)
            nc.gpsimd.memset(ones[:], 1.0).then_inc(cleared_pool, 1)
            pool.wait_ge(cleared_pool, 3)
            pool.wait_ge(var_ready, 1)
            nc.gpsimd.tensor_tensor(norm_all[:, :, 1], var_eps[:], minus_half[:], ALU.pow).then_inc(rstd_ready, 1)

            steps_due = pool.alloc_register("steps_due")
            pool.reg_mov(steps_due, 1)

            def carry_k(G, u, par):
                if isinstance(u, int) and u < 2:
                    pool.wait_ge(s_made, G * (4 * QUADS))
                else:
                    pool.wait_ge(s_made, 4 * (quad_no(G, u) - 1))
                pool.wait_ge(k_ready, steps_due)
                pool.reg_add(steps_due, steps_due, 1)
                nc.gpsimd.tensor_copy(k_win[:, par, :, 0:2 * BLOCK, :],
                                      k_win[:, 1 - par, :, 4 * BLOCK:, :]).then_inc(k_carried, 1)

            def norms(G, t, par, i):
                J = quad_no(G, t)
                pool.wait_ge(inverted, J * 4 + i + 1)
                for r in range(2):
                    n = 2 * i + r
                    w = window(par, i, r)
                    nc.gpsimd.tensor_tensor(w, w, inv_sum[:, par, n:n + 1].unsqueeze(2).to_broadcast([PARTS, WIN, WIN]),
                                            ALU.mult).then_inc(normed, 1)

            def prologue(G):
                for u in range(2):
                    carry_k(G, u, u)

            def body(G, t, par):
                for i in range(4):
                    norms(G, t, par, i)
                if not last(t):
                    carry_k(G, t + 2, par)

            with pool.Fori(0, ALL_STRIPS) as G:
                over_strip(pool, G, prologue, body, lambda G: None)

        @block.vector
        def _(dve):
            chain = [0]

            def then(ins):
                chain[0] += 1
                ins.then_inc(dve_step, 1)
                dve.wait_ge(dve_step, chain[0])

            nc.vector.memset(probs[:], 0.0)
            for b in range(BATCH):
                with dve.Fori(0, STAT_LOADS // 2) as n:
                    for par in range(2):
                        dve.wait_ge(stat_loaded[par], (n + (b * STAT_LOADS // 2 + 1)) * 16)
                        for k in range(STAT_PIECES):
                            at = (n * 2 + (b * STAT_LOADS + par)) * STAT_PIECES + k
                            ins = nc.vector.bn_stats(
                                stats[:, bass.ds(at, 1), :].rearrange("p a s -> p (a s)"),
                                stat_in[:, par, k * STAT_PIECE:(k + 1) * STAT_PIECE])
                        ins.then_inc(stat_read[par], 1)
            then(nc.vector.memset(var_eps[:], 0.0))
            for b in range(BATCH):
                n = STAT_LOADS * STAT_PIECES
                then(nc.vector.bn_aggr(moments[:, b, :], stats[:, b * n:(b + 1) * n, :].rearrange("p a s -> p (a s)")))
            then(nc.vector.tensor_tensor(var_eps[:], moments[:, :, 0], moments[:, :, 0], ALU.mult))
            nc.vector.tensor_tensor(moments[:, :, 1], moments[:, :, 1], var_eps[:], ALU.add).then_inc(avg_in, 1)
            dve.wait_ge(avg_out, 1)
            avg = o_bank[:, 0:2 * BATCH].rearrange("p (b m) -> p b m", m=2)
            then(nc.vector.tensor_copy(norm_all[:, :, 0], avg[:, :, 0]))
            then(nc.vector.tensor_tensor(var_eps[:], norm_all[:, :, 0], norm_all[:, :, 0], ALU.mult))
            then(nc.vector.tensor_tensor(var_eps[:], avg[:, :, 1], var_eps[:], ALU.subtract))
            nc.vector.tensor_scalar(var_eps[:], var_eps[:], EPS, None, ALU.add).then_inc(var_ready, 1)

            dve.wait_ge(bias_in, 16 * N_BIAS)
            for row in range(2):
                for blocked in range(2):
                    variant = 1 - blocked if row == 0 else blocked
                    for col in range(3):
                        then(nc.vector.tensor_copy(bias_all[:, row, variant, col], bias_raw[:]))
                    tables = bias_all[:, row, variant]
                    edge = tables[:, 0, 0:BLOCK, :]
                    then(nc.vector.tensor_scalar(edge, edge, BLOCKED, None, ALU.add))
                    edge = tables[:, 2, WIN - BLOCK:, :]
                    then(nc.vector.tensor_scalar(edge, edge, BLOCKED, None, ALU.add))
                    if blocked:
                        rows = slice(0, BLOCK) if row == 0 else slice(WIN - BLOCK, WIN)
                        edge = tables[:, :, :, rows].rearrange("p c w h -> p (c w) h")
                        then(nc.vector.tensor_scalar(edge, edge, BLOCKED, None, ALU.add))
            dve.wait_ge(rstd_ready, 1)
            dve.wait_ge(loaded_const, 16 * N_CONST)
            before = chain[0]
            columns_due = dve.alloc_register("columns_due")
            dve.reg_mov(columns_due, 1)

            def normalise(G, u, par):
                U = step_no(G, u)
                if isinstance(u, int) and u < 2:
                    dve.wait_ge(x_loaded, G * 16 + 16)
                    dve.wait_ge(v_made, G * STEPS)
                else:
                    dve.wait_ge(v_made, U - 1)
                src = x_strip[:, bass.ds(G % 2, 1), :, bass.ds(u * SPAN, SPAN)].rearrange("p a h w -> p w (a h)")
                nc.vector.tensor_scalar(xh[:, par], src, norm_now[:, 0:1], norm_now[:, 1:2],
                                        ALU.subtract, ALU.mult).then_inc(xh_ready, 1)

            def keep_q(G, u, par):
                U = step_no(G, u)
                dve.wait_ge(q_made, U + 1)
                if isinstance(u, int) and u < 2:
                    dve.wait_ge(s_made, G * (4 * QUADS))
                else:
                    dve.wait_ge(s_made, 4 * (quad_no(G, u) - 2) + 1)
                for g in range(HG):
                    ins = nc.vector.tensor_tensor(
                        q_diag[:, par, g].rearrange("p r i (h q) -> p h (r i) q", h=HPG),
                        q_bank[:, g * 128:(g + 1) * 128].rearrange("p (b q) -> p b q", q=QB).unsqueeze(1)
                        .to_broadcast([PARTS, HPG, 8, QB]),
                        head_mask[:].unsqueeze(2).unsqueeze(3).to_broadcast([PARTS, HPG, 8, QB]), ALU.mult)
                ins.then_inc(q_ready, 1)

            def keep_v(G, u, par):
                U = step_no(G, u)
                dve.wait_ge(v_made, U + 1)
                if isinstance(u, int) and u < 2:
                    dve.wait_ge(o_made, quad_no(G, 0))
                else:
                    dve.wait_ge(o_made, quad_no(G, u) - 1)
                nc.vector.tensor_copy(v_sb[:, par].rearrange("p c n -> p (c n)"), v_bank[:]).then_inc(v_ready, 1)

            def add_bias(G, t, par, i):
                J = quad_no(G, t)
                if i == 0:
                    dve.wait_ge(t_made, J * 4 if first(t) else J * 4 - 4)
                dve.wait_ge(s_made, columns_due)
                dve.reg_add(columns_due, columns_due, 1)
                col = 0 if first(t) and i == 0 else 2 if last(t) and i == 3 else 1
                for r in range(2):
                    n = 2 * i + r
                    w = window(par, i, r)
                    nc.vector.tensor_tensor_reduce(
                        out=w, in0=s_bank[i % 2][:, 144 * r:144 * (r + 1)].rearrange("p (w h) -> p w h", h=WIN),
                        in1=bias_now[:, r, col], scale=1.0, scalar=BIG, op0=ALU.add, op1=ALU.min,
                        accum_out=minus_max[:, par, n:n + 1]).then_inc(biased, 1)

            def invert(G, t, par, i):
                dve.wait_ge(exp_done, quad_no(G, t) * 8 + 2 * i + 2)
                nc.vector.reciprocal(inv_sum[:, par, 2 * i:2 * i + 2],
                                     row_sum[:, par, 2 * i:2 * i + 2]).then_inc(inverted, 1)

            def keep_pt(G, t, par, i):
                J = quad_no(G, t)
                dve.wait_ge(t_made, J * 4 + i + 1)
                nc.vector.tensor_copy(pt_sb[:, par, i].rearrange("p r s c -> p (r s c)"),
                                      t_bank[i % 2][:]).then_inc(pt_dve, 1)

            def residual(G, t):
                J = quad_no(G, t)
                dve.wait_ge(y_made, J + 1)
                x_in = x_strip[:, bass.ds(G % 2, 1), BLOCK:BLOCK + STRIP, bass.ds(t * SPAN + PAD, SPAN)]
                nc.vector.scalar_tensor_tensor(
                    out=y_strip[:, :, bass.ds(t * SPAN, SPAN)],
                    in0=o_bank[:, 256:384].rearrange("p (h w) -> p h w", w=SPAN), scalar=b_out[:],
                    in1=x_in.rearrange("p a h w -> p (a h) w"), op0=ALU.add, op1=ALU.add).then_inc(y_ready, 1)

            def prologue(G):
                g = G % STRIPS
                dve.wait_ge(biased, G * (8 * QUADS))
                dve.wait_ge(xh_ready, G * STEPS)
                nc.vector.tensor_copy(norm_now[:], norm_all[:, bass.ds(G // STRIPS, 1), :].rearrange(
                    "p a s -> p (a s)")).then_inc(dve_step, 1)
                for row, variant in ((0, (g + (STRIPS - 1)) // STRIPS), (1, (g + 1) // STRIPS)):
                    nc.vector.tensor_copy(
                        bias_now[:, row].rearrange("p c h w -> p (c h w)"),
                        bias_all[:, row, bass.ds(variant, 1)].rearrange("p a c h w -> p (a c h w)")).then_inc(dve_step, 1)
                dve.wait_ge(dve_step, G * 3 + (before + 3))
                normalise(G, 0, 0)
                normalise(G, 1, 1)
                keep_q(G, 0, 0)
                keep_q(G, 1, 1)
                keep_v(G, 0, 0)

            def body(G, t, par):
                if not last(t):
                    normalise(G, t + 2, par)
                for i in range(4):
                    add_bias(G, t, par, i)
                    if i:
                        invert(G, t, par, i - 1)
                    if not first(t) and i % 2 == 1:
                        keep_pt(G, t - 1, 1 - par, i)
                invert(G, t, par, 3)
                if not last(t):
                    keep_q(G, t + 2, par)
                if first(t):
                    dve.wait_ge(y_stored, G * 16)
                keep_v(G, t + 1, 1 - par)
                if not first(t):
                    residual(G, t - 1)

            def drain(G):
                keep_pt(G, QUADS - 1, 1, 1)
                keep_pt(G, QUADS - 1, 1, 3)
                residual(G, QUADS - 1)

            with dve.Fori(0, ALL_STRIPS) as G:
                over_strip(dve, G, prologue, body, drain)


def kernel(x, L0_conv_w_in, L0_conv_b_in, L0_conv_w_out, L0_conv_b_out, L0_conv_pce):
    import numpy as np
    import concourse.bacc as bacc
    from concourse.bass_utils import run_bass_kernel_spmd

    x, w_in, b_in, w_out, b_out, pce = (
        np.asarray(a) for a in (x, L0_conv_w_in, L0_conv_b_in, L0_conv_w_out, L0_conv_b_out, L0_conv_pce))
    head_of = np.arange(PARTS) // HEAD_DIM
    group_of = np.arange(PARTS) // GROUP_CH
    arrays = {
        "x_d": np.ascontiguousarray(x),
        "w_in_d": np.ascontiguousarray(w_in.T),
        "b_in_d": np.ascontiguousarray(b_in.reshape(-1, PARTS).T),
        "b_q_d": np.ascontiguousarray(b_in[:HG * PARTS].reshape(1, -1)),
        "w_out_d": np.ascontiguousarray(w_out.T.reshape(HG, PARTS, CH).transpose(1, 0, 2)),
        "b_out_d": np.ascontiguousarray(b_out.reshape(CH, 1)),
        "pce_d": np.ascontiguousarray(pce),
        "ident_d": np.eye(PARTS, dtype=np.float32),
        "group_avg_d": (group_of[:, None] == group_of[None, :]).astype(np.float32) / GROUP_CH,
        "head_mask_d": np.where(head_of[:, None] == np.arange(HPG)[None, :], np.float32(-SCALE), np.float32(0)),
    }
    nc = bacc.Bacc("TRN2", target_bir_lowering=False, num_devices=1)
    aps = {n: nc.dram_tensor(n, a.shape, mybir.dt.float32, kind="ExternalInput").ap() for n, a in arrays.items()}
    out = nc.dram_tensor("out_d", x.shape, mybir.dt.float32, kind="ExternalOutput").ap()
    build(nc, aps["x_d"], aps["w_in_d"], aps["b_in_d"], aps["b_q_d"], aps["w_out_d"], aps["b_out_d"], aps["pce_d"],
          aps["ident_d"], aps["group_avg_d"], aps["head_mask_d"], out)
    r = run_bass_kernel_spmd(nc, [arrays], core_ids=[0])
    return r.results[0]["out_d"]
```

```python
from contextlib import ExitStack

import concourse.bass as bass
from concourse import mybir
from concourse.alu_op_type import AluOpType as ALU

BATCH, CH, HEIGHT, WIDTH = 2, 128, 256, 256
HEADS, HEAD_DIM, BLOCK = 8, 32, 4
GROUP_CH = 4
EPS = 1e-5
SCALE = HEAD_DIM ** -0.5
PARTS = 128
HG = 2
HPG = HEADS // HG
QB = BLOCK * BLOCK
WIN = 3 * BLOCK
STRIP = 2 * BLOCK
KROWS = STRIP + 2 * BLOCK
STRIPS = HEIGHT // STRIP
ALL_STRIPS = BATCH * STRIPS
QUADS = WIDTH // (4 * BLOCK)
STEPS = QUADS + 1
SPAN = 4 * BLOCK
PAD = 3 * BLOCK
XCOLS = STEPS * SPAN
PLAIN_ROWS, BLOCKED_ROWS = 0, 1
BLOCKED = 1.0e30
BIG = 3.0e38
PRE_PIECES = 4
STAT_ROWS = 16
STAT_LOADS = HEIGHT // STAT_ROWS
STAT_PIECE = 512
STAT_PIECES = STAT_ROWS * WIDTH // STAT_PIECE


def build(nc, x, w_in_t, b_in_c, w_out_t, b_out_c, pce, ident_d, group_avg_d, head_mask_d, out):
    f32 = mybir.dt.float32
    f32r = mybir.dt.float32r
    ACT = mybir.ActivationFunctionType

    ctx = ExitStack()
    with ctx:
        def sb(name, shape, dtype=f32):
            return ctx.enter_context(nc.sbuf_tensor(name, shape, dtype))

        def pb(name):
            return ctx.enter_context(nc.psum_tensor(name, [PARTS, 512], f32))

        def sem(name):
            return ctx.enter_context(nc.semaphore(name))

        w_in = sb("w_in", [PARTS, 3 * HEADS * HEAD_DIM])
        w_v = sb("w_v", [PARTS, 2, HEADS * HEAD_DIM], f32r)
        w_out = sb("w_out", [PARTS, HG, CH])
        b_in = sb("b_in", [PARTS, 3 * HG])
        b_out = sb("b_out", [PARTS, 1])
        ident = sb("ident", [PARTS, PARTS])
        group_avg = sb("group_avg", [PARTS, PARTS])
        head_mask = sb("head_mask", [PARTS, HPG])
        stats = sb("stats", [PARTS, BATCH * STAT_LOADS * STAT_PIECES, 6])
        stat_in = sb("stat_in", [PARTS, 2, STAT_ROWS * WIDTH])
        moments = sb("moments", [PARTS, BATCH, 2])
        var_eps = sb("var_eps", [PARTS, BATCH])
        minus_half = sb("minus_half", [PARTS, BATCH])
        norm_all = sb("norm_all", [PARTS, BATCH, 2])
        norm_now = sb("norm_now", [PARTS, 2])
        bias_raw = sb("bias_raw", [PARTS, WIN, WIN])
        bias_all = sb("bias_all", [PARTS, 2, 2, 3, WIN, WIN])
        x_strip = sb("x_strip", [PARTS, 2, KROWS, XCOLS])
        y_strip = sb("y_strip", [PARTS, 2, STRIP, WIDTH])
        xh = sb("xh", [PARTS, 3, SPAN, KROWS])
        xh_parts = sb("xh_parts", [PARTS, 3, 2, SPAN, KROWS], f32r)
        k_keep = sb("k_keep", [PARTS, HG, XCOLS, STRIP])
        k_win = sb("k_win", [PARTS, 3, HG, 6 * BLOCK, KROWS])
        v_sb = sb("v_sb", [PARTS, 2, 2, HEADS * HEAD_DIM])
        v_first = sb("v_first", [PARTS, HEADS * HEAD_DIM])
        pre_x = stat_in[:, 0, 0:XCOLS * STRIP]
        q_lin = sb("q_lin", [PARTS, HG, 8 * QB])
        q_diag = sb("q_diag", [PARTS, 3, HG, 2, 4, HPG * QB])
        probs = sb("probs", [PARTS, 2, 4, 2, 4 * BLOCK, KROWS])
        minus_max = sb("minus_max", [PARTS, 2, 8])
        row_sum = sb("row_sum", [PARTS, 2, 8])
        inv_sum = sb("inv_sum", [PARTS, 2, 8])
        pt_sb = sb("pt_sb", [PARTS, 2, 4, 2, 2, PARTS])
        o_sb = sb("o_sb", [PARTS, HG, 8 * QB])

        k_bank, v_bank, q_bank, o_bank = pb("k_bank"), pb("v_bank"), pb("q_bank"), pb("o_bank")
        s_bank = [pb("s_bank0"), pb("s_bank1")]
        t_bank = [pb("t_bank0"), pb("t_bank1")]

        loaded_const = sem("loaded_const")
        bias_in = sem("bias_in")
        stat_loaded = [sem("stat_loaded0"), sem("stat_loaded1")]
        stat_read = [sem("stat_read0"), sem("stat_read1")]
        dve_step = sem("dve_step")
        avg_in, avg_out, var_ready, rstd_ready = sem("avg_in"), sem("avg_out"), sem("var_ready"), sem("rstd_ready")
        cleared_pool = sem("cleared_pool")
        x_loaded = sem("x_loaded")
        y_stored = sem("y_stored")
        xh_ready = sem("xh_ready")
        xh_rounded, xh_split = sem("xh_rounded"), sem("xh_split")
        k_made, k_ready, k_carried = sem("k_made"), sem("k_ready"), sem("k_carried")
        k_upper, k_filled = sem("k_upper"), sem("k_filled")
        pre_xh, pre_made, pre_kept = sem("pre_xh"), sem("pre_made"), sem("pre_kept")
        q_made, q_biased, q_ready = sem("q_made"), sem("q_biased"), sem("q_ready")
        v_made, v_ready = sem("v_made"), sem("v_ready")
        s_made = sem("s_made")
        biased = sem("biased")
        exp_done = sem("exp_done")
        inverted = sem("inverted")
        normed = sem("normed")
        t_made = sem("t_made")
        pt_act, pt_dve = sem("pt_act"), sem("pt_dve")
        o_made, o_ready, y_made, y_ready = sem("o_made"), sem("o_ready"), sem("y_made"), sem("y_ready")

        N_CONST = 7
        N_BIAS = QB

        START = 32

        def at(n):
            return n + START

        def step_no(G, u):
            return G * STEPS + u

        def quad_no(G, t):
            return G * QUADS + t

        def before(G, t):
            return (G - 1, QUADS - 1) if isinstance(t, int) and t == 0 else (G, t - 1)

        def buf(u):
            return 2 if u == 0 else u % 2

        def over_images(eng, image_start, body, drain):
            def strip(G, row_kinds, prev, then):
                body(G, 0, 0, row_kinds, prev, then)
                with eng.Fori(0, QUADS // 2 - 1) as k:
                    body(G, k * 2 + 1, 1, row_kinds, True, then)
                    body(G, k * 2 + 2, 0, row_kinds, True, then)
                body(G, QUADS - 1, 1, row_kinds, True, then)

            with eng.Fori(0, BATCH) as b:
                base = b * STRIPS
                image_start(b, base)
                strip(base, (BLOCKED_ROWS, PLAIN_ROWS), False, True)
                with eng.Fori(1, STRIPS - 1) as g:
                    strip(base + g, (PLAIN_ROWS, PLAIN_ROWS), True, True)
                strip(base + (STRIPS - 1), (PLAIN_ROWS, BLOCKED_ROWS), True, False)
                drain(base + (STRIPS - 1))

        def window(par, i, r):
            return probs[:, par, i, r, BLOCK * (i % 2):BLOCK * (i % 2) + WIN, BLOCK * r:BLOCK * r + WIN]

        first = lambda t: isinstance(t, int) and t == 0
        last = lambda t: isinstance(t, int) and t == QUADS - 1
        PRE_COLS = XCOLS * STRIP // (2 * PRE_PIECES)

        block = ctx.enter_context(nc.Block())

        @block.sync
        def _(sp):
            for produced in (x_loaded, y_stored):
                sp.sem_inc(produced, START)
            for dst, src in ((w_in[:], w_in_t), (w_out[:], w_out_t), (b_in[:], b_in_c), (b_out[:], b_out_c),
                             (ident[:], ident_d), (group_avg[:], group_avg_d), (head_mask[:], head_mask_d)):
                sp.dma_start(dst, src).then_inc(loaded_const, 16)
            for b in range(BATCH):
                with sp.Fori(0, STAT_LOADS // 2) as n:
                    for par in range(2):
                        sp.wait_ge(stat_read[par], at(n + b * STAT_LOADS // 2))
                        src = x[b, :, bass.ds((n * 2 + par) * STAT_ROWS, STAT_ROWS), :]
                        sp.dma_start(stat_in[:, par, :], src.rearrange("c h w -> c (h w)")).then_inc(stat_loaded[par], 16)

            def load(G, b, row0, rows, to_row):
                sp.wait_ge(y_ready, at(quad_no(G - 1, 0)))
                sp.wait_ge(x_loaded, at(G * 16))
                sp.dma_start(x_strip[:, bass.ds(G % 2, 1), to_row:to_row + rows, PAD:PAD + WIDTH]
                             .rearrange("c a h w -> c (a h) w"),
                             x[bass.ds(b, 1), :, bass.ds(row0, rows), :].rearrange("b c h w -> (b c) h w")
                             ).then_inc(x_loaded, 16)

            def store(G, b, g):
                sp.wait_ge(y_ready, at(quad_no(G + 1, 0)))
                sp.dma_start(out[bass.ds(b, 1), :, bass.ds(g * STRIP, STRIP), :].rearrange("b c h w -> (b c) (h w)"),
                             y_strip[:, bass.ds(G % 2, 1)].rearrange("c a h w -> c (a h w)")).then_inc(y_stored, 16)

            sp.wait_ge(cleared_pool, 1)
            with sp.Fori(0, BATCH) as b:
                base = b * STRIPS
                load(base, b, 0, KROWS - BLOCK, BLOCK)
                with sp.Fori(0, STRIPS - 2) as g:
                    load(base + (g + 1), b, g * STRIP + (STRIP - BLOCK), KROWS, 0)
                    store(base + g, b, g)
                load(base + (STRIPS - 1), b, HEIGHT - KROWS + BLOCK, KROWS - BLOCK, 0)
                store(base + (STRIPS - 2), b, STRIPS - 2)
                store(base + (STRIPS - 1), b, STRIPS - 1)
            sp.wait_ge(y_stored, at(16 * ALL_STRIPS))

        @block.tensor
        def _(pe):
            for made in (k_made, q_made, v_made, s_made, t_made, o_made, y_made, pre_made):
                pe.sem_inc(made, START)
            pe.wait_ge(loaded_const, 16 * N_CONST)
            pe.wait_ge(avg_in, 1)
            nc.tensor.matmul(o_bank[:, 0:2 * BATCH], group_avg[:], moments[:].rearrange("p b m -> p (b m)"),
                             start=True, stop=True).then_inc(avg_out, 1)

            def project_k(G, u, x_buf):
                pe.wait_ge(xh_ready, at(step_no(G, u) + 1))
                if isinstance(u, int) and u <= 1:
                    pe.wait_ge(k_ready, at(step_no(G, u)))
                for g in range(HG):
                    c0 = (HG + g) * PARTS
                    mm = nc.tensor.matmul(k_bank[:, g * 128:(g + 1) * 128], w_in[:, c0:c0 + PARTS],
                                          xh[:, x_buf, :, STRIP:], start=True, stop=True)
                mm.then_inc(k_made, 1)

            def project_q(G, u, x_buf):
                if isinstance(u, int) and u <= 1:
                    pe.wait_ge(q_biased, at(step_no(G, u)))
                xq = xh[:, x_buf, :, BLOCK:BLOCK + STRIP].rearrange("p w (r h) -> p r w h", h=BLOCK)
                for g in range(HG):
                    mm = nc.tensor.matmul(q_bank[:, g * 128:(g + 1) * 128], w_in[:, g * PARTS:(g + 1) * PARTS],
                                          xq, start=True, stop=True)
                mm.then_inc(q_made, 1)

            def project_v(G, u, x_buf):
                if isinstance(u, int) and u <= 1:
                    pe.wait_ge(v_ready, at(step_no(G, u)))
                pe.wait_ge(xh_split, at(step_no(G, u) + 1))
                for c in range(1 if first(u) else 0, 2):
                    for n, (x_part, w_part) in enumerate(((0, 0), (0, 1), (1, 0))):
                        mm = nc.tensor.matmul(
                            v_bank[:, c * 256:(c + 1) * 256],
                            xh_parts[:, x_buf, x_part, c * 8:(c + 1) * 8, :].rearrange("p w h -> p (w h)"),
                            w_v[:, w_part], start=n == 0, stop=n == 2)
                mm.then_inc(v_made, 1)

            def scores(G, t, par, i):
                J = quad_no(G, t)
                if i == 0:
                    pe.wait_ge(k_filled, at(step_no(G, t) + 2))
                if i <= 1:
                    pe.wait_ge(q_ready, at(step_no(G, t) + 1 + i))
                if i > 0:
                    pe.wait_ge(biased, at(J * 8 + 2 * (i - 1)))
                this, after = 2 if first(t) else par, 1 - par
                for r in range(2):
                    for g in range(HG):
                        mm = nc.tensor.matmul(
                            s_bank[i % 2][64 * g:64 * (g + 1), 144 * r:144 * (r + 1)],
                            q_diag[:, this, g, r, 3] if i == 0 else q_diag[:, after, g, r, i - 1],
                            k_win[:, par, g, BLOCK * i:BLOCK * i + WIN, BLOCK * r:BLOCK * r + WIN],
                            start=True, stop=True)
                mm.then_inc(s_made, 1)

            def transposes(G, t, par, i):
                J = quad_no(G, t)
                pe.wait_ge(normed, at(J * 8 + 2 * i + 2))
                if i >= 2:
                    pe.wait_ge(pt_act, at(J * 2 + i - 1))
                for r in range(2):
                    for slot in range(2):
                        half = 1 - slot if i < 2 else slot
                        mm = nc.tensor.transpose(t_bank[i % 2][:, (2 * r + slot) * 128:(2 * r + slot + 1) * 128],
                                                 probs[:, par, i, r, half * 8:(half + 1) * 8, :].rearrange("p w h -> p (w h)"),
                                                 ident[:])
                mm.then_inc(t_made, 1)

            def weigh_v(G, t, par):
                J = quad_no(G, t)
                pe.wait_ge(pt_dve, at(J * 2 + 2))
                this, after = par, 1 - par
                for g in range(HG):
                    for v, i0, i1, slot in ((v_sb[:, after, 0], 0, 4, 0),
                                            (v_sb[:, this, 1], 0, 2, 1),
                                            (v_sb[:, after, 1], 2, 4, 1)):
                        for h in range(HPG):
                            c0 = (g * HPG + h) * QB
                            p = pt_sb[:, par, i0:i1, :, slot, c0:c0 + QB].rearrange("p i r q -> p r i q")
                            o = o_bank[32 * h:32 * (h + 1), g * 128:(g + 1) * 128].rearrange("p (r i q) -> p r i q", r=2, i=4)
                            mm = nc.tensor.matmul(
                                o[:, :, i0:i1, :],
                                v[:, (g * HPG + h) * HEAD_DIM:(g * HPG + h + 1) * HEAD_DIM], p,
                                start=slot == 0, stop=i0 == 2)
                mm.then_inc(o_made, 1)

            def project_out(G, t, par):
                pe.wait_ge(o_ready, at(quad_no(G, t) + 1))
                for g in range(HG):
                    o = o_sb[:, g].rearrange("p (r iw h) -> p r h iw", r=2, h=BLOCK)
                    mm = nc.tensor.matmul(o_bank[:, 256:384], w_out[:, g], o, start=g == 0, stop=g == HG - 1)
                mm.then_inc(y_made, 1)

            def image_start(b, G):
                pe.wait_ge(pre_xh, at(b + 1))
                pe.wait_ge(k_ready, at(step_no(G, 0)))
                pe.wait_ge(v_ready, at(step_no(G, 0)))
                for n in range(2 * PRE_PIECES * HG):
                    piece, g = n // HG, n % HG
                    c0 = (HG + g) * PARTS
                    pe.wait_ge(pre_kept, at(b * (2 * PRE_PIECES * HG) + (n - 1)))
                    nc.tensor.matmul((k_bank, v_bank)[n % 2][:, 0:PRE_COLS], w_in[:, c0:c0 + PARTS],
                                     pre_x[:, piece * PRE_COLS:(piece + 1) * PRE_COLS],
                                     start=True, stop=True).then_inc(pre_made, 1)
                pe.wait_ge(pre_kept, at(b * (2 * PRE_PIECES * HG) + 2 * PRE_PIECES * HG))
                for u in range(2):
                    project_k(G, u, buf(u))
                    project_q(G, u, buf(u))

            def body(G, t, par, row_kinds, prev, then):
                G1, t1 = before(G, t)
                scores(G, t, par, 0)
                if prev or not first(t):
                    transposes(G1, t1, 1 - par, 0)
                    transposes(G1, t1, 1 - par, 1)
                if first(t):
                    project_v(G, 0, buf(0))
                scores(G, t, par, 1)
                if prev or not first(t):
                    transposes(G1, t1, 1 - par, 2)
                    transposes(G1, t1, 1 - par, 3)
                if not last(t):
                    project_k(G, t + 2, par)
                    project_q(G, t + 2, par)
                elif then:
                    project_k(G + 1, 0, buf(0))
                    project_q(G + 1, 0, buf(0))
                scores(G, t, par, 2)
                if prev or not first(t):
                    weigh_v(G1, t1, 1 - par)
                if last(t) and then:
                    project_k(G + 1, 1, buf(1))
                    project_q(G + 1, 1, buf(1))
                scores(G, t, par, 3)
                project_v(G, t + 1, 1 - par)
                if prev or not first(t):
                    project_out(G1, t1, 1 - par)

            def drain(G):
                for i in range(4):
                    transposes(G, QUADS - 1, 1, i)
                weigh_v(G, QUADS - 1, 1)
                project_out(G, QUADS - 1, 1)

            over_images(pe, image_start, body, drain)

        @block.scalar
        def _(act):
            for q in range(QB):
                ww, hh = q // BLOCK, q % BLOCK
                src = bass.AP(pce.tensor, 16 * (BLOCK - ww) + (BLOCK - hh), [[256, HEADS], [16, WIN], [1, WIN]])
                act.dma_start(bias_raw[q::QB], src).then_inc(bias_in, 16)

            act.wait_ge(loaded_const, 16 * N_CONST)

            for produced in (k_ready, q_biased, exp_done, pt_act, o_ready, pre_kept):
                act.sem_inc(produced, START)

            def keep_k(G, u, win):
                U = step_no(G, u)
                act.wait_ge(k_made, at(U + 1))
                act.wait_ge(s_made, at(4 * (quad_no(G, u) - 2)))
                act.wait_ge(k_carried, at(U - 1))
                for g in range(HG):
                    ins = nc.scalar.activation(
                        k_win[:, win, g, 2 * BLOCK:, STRIP:],
                        k_bank[:, g * 128:(g + 1) * 128].rearrange("p (w h) -> p w h", h=STRIP),
                        ACT.Identity, bias=b_in[:, HG + g:HG + g + 1])
                ins.then_inc(k_ready, 1)

            def bias_q(G, u):
                act.wait_ge(q_made, at(step_no(G, u) + 1))
                act.wait_ge(q_ready, at(step_no(G, u)))
                for g in range(HG):
                    ins = nc.scalar.activation(q_lin[:, g], q_bank[:, g * 128:(g + 1) * 128],
                                               ACT.Identity, bias=b_in[:, g:g + 1])
                ins.then_inc(q_biased, 1)

            def exps(G, t, par, i):
                J = quad_no(G, t)
                for r in range(2):
                    n = 2 * i + r
                    act.wait_ge(biased, at(J * 8 + n + 1))
                    w = window(par, i, r)
                    nc.scalar.activation(w, w, ACT.Exp, bias=minus_max[:, par, n:n + 1], scale=-1.0,
                                         accum_out=row_sum[:, par, n:n + 1]).then_inc(exp_done, 1)

            def keep_pt(G, t, par, i):
                act.wait_ge(t_made, at(quad_no(G, t) * 4 + i + 1))
                nc.scalar.activation(pt_sb[:, par, i].rearrange("p r s c -> p (r s c)"), t_bank[i % 2][:],
                                     ACT.Identity).then_inc(pt_act, 1)

            def keep_o(G, t):
                J = quad_no(G, t)
                act.wait_ge(o_made, at(J + 1))
                act.wait_ge(y_made, at(J))
                for g in range(HG):
                    ins = nc.scalar.activation(o_sb[:, g], o_bank[:, g * 128:(g + 1) * 128], ACT.Identity,
                                               bias=b_in[:, 2 * HG + g:2 * HG + g + 1])
                ins.then_inc(o_ready, 1)

            def image_start(b, G):
                act.wait_ge(k_filled, at(step_no(G, 0)))
                for n in range(2 * PRE_PIECES * HG):
                    piece, g = n // HG, n % HG
                    act.wait_ge(pre_made, at(b * (2 * PRE_PIECES * HG) + (n + 1)))
                    keep = k_keep[:, g].rearrange("p w h -> p (w h)")
                    nc.scalar.activation(keep[:, piece * PRE_COLS:(piece + 1) * PRE_COLS],
                                         (k_bank, v_bank)[n % 2][:, 0:PRE_COLS], ACT.Identity,
                                         bias=b_in[:, HG + g:HG + g + 1]).then_inc(pre_kept, 1)
                keep_k(G, 0, 2)
                bias_q(G, 0)
                keep_k(G, 1, 0)
                bias_q(G, 1)

            def body(G, t, par, row_kinds, prev, then):
                G1, t1 = before(G, t)
                if prev or not first(t):
                    keep_pt(G1, t1, 1 - par, 0)
                    keep_pt(G1, t1, 1 - par, 1)
                exps(G, t, par, 0)
                exps(G, t, par, 1)
                if not last(t):
                    keep_k(G, t + 2, 1 - par)
                    bias_q(G, t + 2)
                elif then:
                    keep_k(G + 1, 0, 2)
                    bias_q(G + 1, 0)
                exps(G, t, par, 2)
                if prev or not first(t):
                    keep_o(G1, t1)
                if last(t) and then:
                    keep_k(G + 1, 1, 0)
                    bias_q(G + 1, 1)
                exps(G, t, par, 3)

            def drain(G):
                keep_pt(G, QUADS - 1, 1, 0)
                keep_pt(G, QUADS - 1, 1, 1)
                keep_o(G, QUADS - 1)

            over_images(act, image_start, body, drain)

        @block.gpsimd
        def _(pool):
            nc.gpsimd.memset(x_strip[:], 0.0).then_inc(cleared_pool, 1)
            nc.gpsimd.memset(minus_half[:], -0.5).then_inc(cleared_pool, 1)
            pool.wait_ge(cleared_pool, 2)
            pool.wait_ge(var_ready, 1)
            nc.gpsimd.tensor_tensor(norm_all[:, :, 1], var_eps[:], minus_half[:], ALU.pow).then_inc(rstd_ready, 1)

            for produced in (q_ready, normed):
                pool.sem_inc(produced, START)

            def spread_q(G, u, par):
                U = step_no(G, u)
                pool.wait_ge(q_biased, at(U + 1))
                pool.wait_ge(s_made, at(4 * (quad_no(G, u) - 2) + 1))
                for g in range(HG):
                    ins = nc.gpsimd.tensor_tensor(
                        q_diag[:, par, g].rearrange("p r i (h q) -> p h (r i) q", h=HPG),
                        q_lin[:, g].rearrange("p (b q) -> p b q", q=QB).unsqueeze(1).to_broadcast([PARTS, HPG, 8, QB]),
                        head_mask[:].unsqueeze(2).unsqueeze(3).to_broadcast([PARTS, HPG, 8, QB]), ALU.mult)
                ins.then_inc(q_ready, 1)

            def norms(G, t, par, i):
                pool.wait_ge(inverted, at(quad_no(G, t) * 4 + i + 1))
                for r in range(2):
                    n = 2 * i + r
                    w = window(par, i, r)
                    nc.gpsimd.tensor_tensor(w, w, inv_sum[:, par, n:n + 1].unsqueeze(2).to_broadcast([PARTS, WIN, WIN]),
                                            ALU.mult).then_inc(normed, 1)

            def image_start(b, G):
                for u in range(2):
                    spread_q(G, u, buf(u))

            def body(G, t, par, row_kinds, prev, then):
                norms(G, t, par, 0)
                if not last(t):
                    spread_q(G, t + 2, par)
                elif then:
                    spread_q(G + 1, 0, buf(0))
                norms(G, t, par, 1)
                if last(t) and then:
                    spread_q(G + 1, 1, buf(1))
                norms(G, t, par, 2)
                norms(G, t, par, 3)

            over_images(pool, image_start, body, lambda G: None)

        @block.vector
        def _(dve):
            chain = [0]

            def then(ins):
                chain[0] += 1
                ins.then_inc(dve_step, 1)
                dve.wait_ge(dve_step, chain[0])

            for produced in (stat_read[0], stat_read[1], pre_xh, xh_ready, xh_rounded, xh_split, k_upper, k_filled, k_carried,
                             v_ready, biased, inverted, pt_dve, y_ready):
                dve.sem_inc(produced, START)
            nc.vector.memset(probs[:], 0.0)
            def channel_statistics(b):
                with dve.Fori(0, STAT_LOADS // 2) as n:
                    for par in range(2):
                        dve.wait_ge(stat_loaded[par], (n + (b * STAT_LOADS // 2 + 1)) * 16)
                        for k in range(STAT_PIECES):
                            piece = (n * 2 + (b * STAT_LOADS + par)) * STAT_PIECES + k
                            ins = nc.vector.bn_stats(
                                stats[:, bass.ds(piece, 1), :].rearrange("p a s -> p (a s)"),
                                stat_in[:, par, k * STAT_PIECE:(k + 1) * STAT_PIECE])
                        ins.then_inc(stat_read[par], 1)

            channel_statistics(0)
            dve.wait_ge(loaded_const, 16 * N_CONST)
            w_in_v = w_in[:, 2 * HG * PARTS:]
            then(nc.vector.tensor_copy(w_v[:, 0], w_in_v))
            then(nc.vector.tensor_tensor(w_v[:, 1], w_in_v, w_v[:, 0], ALU.subtract))
            dve.wait_ge(bias_in, 16 * N_BIAS)
            for row in range(2):
                for blocked in range(2):
                    variant = BLOCKED_ROWS if blocked else PLAIN_ROWS
                    for col in range(3):
                        then(nc.vector.tensor_copy(bias_all[:, row, variant, col], bias_raw[:]))
                    tables = bias_all[:, row, variant]
                    edge = tables[:, 0, 0:BLOCK, :]
                    then(nc.vector.tensor_scalar(edge, edge, BLOCKED, None, ALU.add))
                    edge = tables[:, 2, WIN - BLOCK:, :]
                    then(nc.vector.tensor_scalar(edge, edge, BLOCKED, None, ALU.add))
                    if blocked:
                        rows = slice(0, BLOCK) if row == 0 else slice(WIN - BLOCK, WIN)
                        edge = tables[:, :, :, rows].rearrange("p c w h -> p (c w) h")
                        then(nc.vector.tensor_scalar(edge, edge, BLOCKED, None, ALU.add))
            channel_statistics(1)
            then(nc.vector.memset(var_eps[:], 0.0))
            for b in range(BATCH):
                n = STAT_LOADS * STAT_PIECES
                then(nc.vector.bn_aggr(moments[:, b, :], stats[:, b * n:(b + 1) * n, :].rearrange("p a s -> p (a s)")))
            then(nc.vector.tensor_tensor(var_eps[:], moments[:, :, 0], moments[:, :, 0], ALU.mult))
            nc.vector.tensor_tensor(moments[:, :, 1], moments[:, :, 1], var_eps[:], ALU.add).then_inc(avg_in, 1)
            dve.wait_ge(avg_out, 1)
            avg = o_bank[:, 0:2 * BATCH].rearrange("p (b m) -> p b m", m=2)
            then(nc.vector.tensor_copy(norm_all[:, :, 0], avg[:, :, 0]))
            then(nc.vector.tensor_tensor(var_eps[:], norm_all[:, :, 0], norm_all[:, :, 0], ALU.mult))
            then(nc.vector.tensor_tensor(var_eps[:], avg[:, :, 1], var_eps[:], ALU.subtract))
            nc.vector.tensor_scalar(var_eps[:], var_eps[:], EPS, None, ALU.add).then_inc(var_ready, 1)

            dve.wait_ge(rstd_ready, 1)
            columns_due = dve.alloc_register("columns_due")
            dve.reg_mov(columns_due, 1 + START)

            def normalise(G, u, x_buf):
                U = step_no(G, u)
                if isinstance(u, int) and u == 0:
                    dve.wait_ge(x_loaded, at(G * 16 + 16))
                dve.wait_ge(v_made, at(U - 2 if isinstance(u, int) and u > 0 else U - 1))
                src = x_strip[:, bass.ds(G % 2, 1), :, bass.ds(u * SPAN, SPAN)].rearrange("p a h w -> p w (a h)")
                nc.vector.tensor_scalar(xh[:, x_buf], src, norm_now[:, 0:1], norm_now[:, 1:2],
                                        ALU.subtract, ALU.mult).then_inc(xh_ready, 1)

            def round_xh(G, u, x_buf):
                dve.wait_ge(xh_ready, at(step_no(G, u) + 1))
                nc.vector.tensor_copy(xh_parts[:, x_buf, 0], xh[:, x_buf]).then_inc(xh_rounded, 1)

            def split_xh(G, u, x_buf):
                dve.wait_ge(xh_rounded, at(step_no(G, u) + 1))
                nc.vector.tensor_tensor(xh_parts[:, x_buf, 1], xh[:, x_buf], xh_parts[:, x_buf, 0],
                                        ALU.subtract).then_inc(xh_split, 1)

            def fill_k(G, u, win):
                dve.wait_ge(s_made, at(4 * (quad_no(G, u) - 2)))
                kept = k_keep[:, :, bass.ds(u * SPAN, SPAN), :]
                nc.vector.tensor_scalar(k_win[:, win, :, 2 * BLOCK:, 0:STRIP], kept, 1.0, None,
                                        ALU.mult).then_inc(k_upper, 1)
                dve.wait_ge(k_upper, at(step_no(G, u) + 1))
                dve.wait_ge(k_ready, at(step_no(G, u) + 1))
                nc.vector.tensor_scalar(kept, k_win[:, win, :, 2 * BLOCK:, STRIP:], 1.0, None,
                                        ALU.mult).then_inc(k_filled, 1)

            def carry_k(G, u, win, to_win):
                dve.wait_ge(s_made, at(4 * (quad_no(G, u) - 1)))
                dve.wait_ge(k_filled, at(step_no(G, u) + 1))
                nc.vector.tensor_copy(k_win[:, to_win, :, 0:2 * BLOCK, :],
                                      k_win[:, win, :, 4 * BLOCK:, :]).then_inc(k_carried, 1)

            def keep_first_v(G):
                dve.wait_ge(v_made, at(step_no(G, 0) + 1))
                nc.vector.tensor_copy(v_first[:], v_bank[:, 256:]).then_inc(v_ready, 1)

            def place_first_v(G):
                dve.wait_ge(v_ready, at(step_no(G, 0) + 1))
                dve.wait_ge(o_made, at(quad_no(G, 0)))
                nc.vector.tensor_copy(v_sb[:, 0, 1], v_first[:])

            def keep_v(G, u, par):
                dve.wait_ge(v_made, at(step_no(G, u) + 1))
                dve.wait_ge(o_made, at(quad_no(G, u) - 1))
                nc.vector.tensor_copy(v_sb[:, par].rearrange("p c n -> p (c n)"), v_bank[:]).then_inc(v_ready, 1)

            def add_bias(G, t, par, i, row_kinds):
                if i == 0:
                    dve.wait_ge(t_made, at(quad_no(G, t) * 4 - 4))
                dve.wait_ge(s_made, columns_due)
                dve.reg_add(columns_due, columns_due, 1)
                col = 0 if first(t) and i == 0 else 2 if last(t) and i == 3 else 1
                for r in range(2):
                    n = 2 * i + r
                    nc.vector.tensor_tensor_reduce(
                        out=window(par, i, r),
                        in0=s_bank[i % 2][:, 144 * r:144 * (r + 1)].rearrange("p (w h) -> p w h", h=WIN),
                        in1=bias_all[:, r, row_kinds[r], col], scale=1.0, scalar=BIG, op0=ALU.add, op1=ALU.min,
                        accum_out=minus_max[:, par, n:n + 1]).then_inc(biased, 1)

            def invert(G, t, par, i):
                dve.wait_ge(exp_done, at(quad_no(G, t) * 8 + 2 * i + 2))
                nc.vector.reciprocal(inv_sum[:, par, 2 * i:2 * i + 2],
                                     row_sum[:, par, 2 * i:2 * i + 2]).then_inc(inverted, 1)

            def keep_pt(G, t, par, i):
                dve.wait_ge(t_made, at(quad_no(G, t) * 4 + i + 1))
                nc.vector.tensor_copy(pt_sb[:, par, i].rearrange("p r s c -> p (r s c)"),
                                      t_bank[i % 2][:]).then_inc(pt_dve, 1)

            def residual(G, t):
                dve.wait_ge(y_made, at(quad_no(G, t) + 1))
                x_in = x_strip[:, bass.ds(G % 2, 1), BLOCK:BLOCK + STRIP, bass.ds(t * SPAN + PAD, SPAN)]
                nc.vector.scalar_tensor_tensor(
                    out=y_strip[:, bass.ds(G % 2, 1), :, bass.ds(t * SPAN, SPAN)].rearrange("p a h w -> p (a h) w"),
                    in0=o_bank[:, 256:384].rearrange("p (h w) -> p h w", w=SPAN), scalar=b_out[:],
                    in1=x_in.rearrange("p a h w -> p (a h) w"), op0=ALU.add, op1=ALU.add).then_inc(y_ready, 1)

            steps_before = chain[0]

            def image_start(b, G):
                dve.wait_ge(xh_ready, at(step_no(G, 0)))
                nc.vector.tensor_scalar(norm_now[:], norm_all[:, bass.ds(b, 1), :].rearrange(
                    "p a s -> p (a s)"), 1.0, None, ALU.mult).then_inc(dve_step, 1)
                dve.wait_ge(dve_step, b + (steps_before + 1))
                dve.wait_ge(x_loaded, at(G * 16 + 16))
                dve.wait_ge(pre_made, at(b * (2 * PRE_PIECES * HG)))
                src = x_strip[:, bass.ds(G % 2, 1), 0:STRIP, :].rearrange("p a h w -> p w (a h)")
                nc.vector.tensor_scalar(pre_x[:].rearrange("p (w h) -> p w h", h=STRIP), src,
                                        norm_now[:, 0:1], norm_now[:, 1:2],
                                        ALU.subtract, ALU.mult).then_inc(pre_xh, 1)
                normalise(G, 0, buf(0))
                normalise(G, 1, buf(1))
                dve.wait_ge(pre_kept, at(b * (2 * PRE_PIECES * HG) + 2 * PRE_PIECES * HG))
                fill_k(G, 0, 2)
                carry_k(G, 0, 2, 0)
                fill_k(G, 1, 0)
                carry_k(G, 1, 0, 1)
                round_xh(G, 0, buf(0))
                split_xh(G, 0, buf(0))
                round_xh(G, 1, buf(1))

            def body(G, t, par, row_kinds, prev, then):
                G1, t1 = before(G, t)
                add_bias(G, t, par, 0, row_kinds)
                if not last(t):
                    normalise(G, t + 2, par)
                elif then:
                    normalise(G + 1, 0, buf(0))
                if first(t):
                    keep_first_v(G)
                add_bias(G, t, par, 1, row_kinds)
                invert(G, t, par, 0)
                if prev or not first(t):
                    keep_pt(G1, t1, 1 - par, 2)
                    keep_pt(G1, t1, 1 - par, 3)
                if not last(t):
                    round_xh(G, t + 2, par)
                elif then:
                    round_xh(G + 1, 0, buf(0))
                add_bias(G, t, par, 2, row_kinds)
                if last(t) and then:
                    normalise(G + 1, 1, buf(1))
                invert(G, t, par, 1)
                if not last(t):
                    fill_k(G, t + 2, 1 - par)
                elif then:
                    fill_k(G + 1, 0, 2)
                    carry_k(G + 1, 0, 2, 0)
                if first(t):
                    split_xh(G, 1, buf(1))
                if not last(t):
                    split_xh(G, t + 2, par)
                elif then:
                    split_xh(G + 1, 0, buf(0))
                if first(t):
                    place_first_v(G)
                add_bias(G, t, par, 3, row_kinds)
                if not last(t):
                    carry_k(G, t + 2, 1 - par, par)
                elif then:
                    fill_k(G + 1, 1, 0)
                    carry_k(G + 1, 1, 0, 1)
                invert(G, t, par, 2)
                if first(t):
                    dve.wait_ge(y_stored, at(G * 16 - 16))
                keep_v(G, t + 1, 1 - par)
                invert(G, t, par, 3)
                if prev or not first(t):
                    residual(G1, t1)
                if last(t) and then:
                    round_xh(G + 1, 1, buf(1))

            def drain(G):
                keep_pt(G, QUADS - 1, 1, 2)
                keep_pt(G, QUADS - 1, 1, 3)
                residual(G, QUADS - 1)

            over_images(dve, image_start, body, drain)


def kernel(x, L0_conv_w_in, L0_conv_b_in, L0_conv_w_out, L0_conv_b_out, L0_conv_pce):
    import numpy as np
    import concourse.bacc as bacc
    from concourse.bass_utils import run_bass_kernel_spmd

    x, w_in, b_in, w_out, b_out, pce = (
        np.asarray(a) for a in (x, L0_conv_w_in, L0_conv_b_in, L0_conv_w_out, L0_conv_b_out, L0_conv_pce))
    head_of = np.arange(PARTS) // HEAD_DIM
    group_of = np.arange(PARTS) // GROUP_CH
    arrays = {
        "x_d": np.ascontiguousarray(x),
        "w_in_d": np.ascontiguousarray(w_in.T),
        "b_in_d": np.ascontiguousarray(b_in.reshape(-1, PARTS).T),
        "w_out_d": np.ascontiguousarray(w_out.T.reshape(HG, PARTS, CH).transpose(1, 0, 2)),
        "b_out_d": np.ascontiguousarray(b_out.reshape(CH, 1)),
        "pce_d": np.ascontiguousarray(pce),
        "ident_d": np.eye(PARTS, dtype=np.float32),
        "group_avg_d": (group_of[:, None] == group_of[None, :]).astype(np.float32) / GROUP_CH,
        "head_mask_d": np.where(head_of[:, None] == np.arange(HPG)[None, :], np.float32(-SCALE), np.float32(0)),
    }
    nc = bacc.Bacc("TRN2", target_bir_lowering=False, num_devices=1)
    aps = {n: nc.dram_tensor(n, a.shape, mybir.dt.float32, kind="ExternalInput").ap() for n, a in arrays.items()}
    out = nc.dram_tensor("out_d", x.shape, mybir.dt.float32, kind="ExternalOutput").ap()
    build(nc, aps["x_d"], aps["w_in_d"], aps["b_in_d"], aps["w_out_d"], aps["b_out_d"], aps["pce_d"],
          aps["ident_d"], aps["group_avg_d"], aps["head_mask_d"], out)
    r = run_bass_kernel_spmd(nc, [arrays], core_ids=[0])
    return r.results[0]["out_d"]
```
